# Optimizing a Trainium2 kernel written in Bass

```python
import numpy as np
import jax
import jax.numpy as jnp

def _softmax(x, axis=-1):
    return jax.nn.softmax(x, axis=axis)

def _gelu(x):
    return jax.nn.gelu(x, approximate=True)

def _silu(x):
    return jax.nn.silu(x)

def _sigmoid(x):
    return jax.nn.sigmoid(x)

def _layernorm(x, axis=-1, eps=1e-05):
    m = jnp.mean(x, axis=axis, keepdims=True)
    v = jnp.var(x, axis=axis, keepdims=True)
    return (x - m) / jnp.sqrt(v + eps)

def _scatter_add(tgt, idx, src, axis=0):
    return tgt.at[idx].add(src)

def _segment_sum(src, seg, n):
    return jax.ops.segment_sum(src, seg, n)
kernel_name = 'mk_seq_postln_d1_jaxref_r8_f6368e'

def setup_inputs(seed: int=0):
    np.random.seed(seed)
    _w = jnp.asarray

    def _L0_attn_setup():
        import jax, jax.numpy as jnp
        import numpy as np
        N_HEAD = 16
        N_EMBD = 128
        key = jax.random.key(seed)
        k1, k2 = jax.random.split(key)
        x = jax.random.normal(k1, (2, 256, N_EMBD), dtype=jnp.float32)
        w_qkv = jax.random.normal(k2, (N_EMBD, 3 * N_EMBD), dtype=jnp.float32) * N_EMBD ** (-0.5)
        return {'x': x, 'w_qkv': w_qkv}
    _L0_attn_in = _L0_attn_setup()

    def _L0_ffn_setup():
        import jax, jax.numpy as jnp
        import numpy as np
        DIM = 128
        HIDDEN = 384
        SCALE = 1.0 / 127.0

        def _dequant(w_int, dtype):
            return w_int.astype(dtype) * jnp.asarray(SCALE, dtype)
        key = jax.random.key(seed)
        k_x, k_g, k_u, k_d = jax.random.split(key, 4)
        x = jax.random.normal(k_x, (4, 256, DIM), dtype=jnp.float32)
        w_gate = jax.random.randint(k_g, (HIDDEN, DIM), -127, 128, dtype=jnp.int32)
        w_up = jax.random.randint(k_u, (HIDDEN, DIM), -127, 128, dtype=jnp.int32)
        w_down = jax.random.randint(k_d, (DIM, HIDDEN), -127, 128, dtype=jnp.int32)
        return {'x': x, 'w_gate': w_gate, 'w_up': w_up, 'w_down': w_down}
    _L0_ffn_in = _L0_ffn_setup()
    _d = {'L0_attn_x': _L0_attn_in['x'], 'L0_attn_w_qkv': _L0_attn_in['w_qkv'], 'L0_ffn_w_gate': _L0_ffn_in['w_gate'], 'L0_ffn_w_up': _L0_ffn_in['w_up'], 'L0_ffn_w_down': _L0_ffn_in['w_down']}
    _x0 = _d['L0_attn_x']
    _d['L0_attn_x'] = jax.random.normal(jax.random.fold_in(jax.random.key(seed), 1), (8, 512, 128), dtype=_x0.dtype)
    del _x0
    return _d

def reference(L0_attn_x, L0_attn_w_qkv, L0_ffn_w_gate, L0_ffn_w_up, L0_ffn_w_down):

    def _L0_attn_ref(x, w_qkv):
        import jax, jax.numpy as jnp
        import numpy as np
        N_HEAD = 16
        N_EMBD = 128
        B, T, C = x.shape
        H = N_HEAD
        D = C // H
        qkv = x @ w_qkv
        q, k, v = jnp.split(qkv, 3, axis=2)
        q = q.reshape(B, T, H, D).transpose(0, 2, 1, 3)
        k = k.reshape(B, T, H, D).transpose(0, 2, 1, 3)
        v = v.reshape(B, T, H, D).transpose(0, 2, 1, 3)
        att = jnp.einsum('bhtd,bhsd->bhts', q, k) / np.sqrt(D).astype(np.float32)
        causal = jnp.tril(jnp.ones((T, T), dtype=bool))
        att = jnp.where(causal, att, -jnp.inf)
        att = jax.nn.softmax(att, axis=-1)
        out = jnp.einsum('bhts,bhsd->bhtd', att, v)
        return out.transpose(0, 2, 1, 3).reshape(B, T, C)

    def _L0_ffn_ref(x, w_gate, w_up, w_down):
        import jax, jax.numpy as jnp
        import numpy as np
        DIM = 128
        HIDDEN = 384
        SCALE = 1.0 / 127.0

        def _dequant(w_int, dtype):
            return w_int.astype(dtype) * jnp.asarray(SCALE, dtype)
        wg = _dequant(w_gate, x.dtype)
        wu = _dequant(w_up, x.dtype)
        wd = _dequant(w_down, x.dtype)
        gate = jnp.einsum('bsd,hd->bsh', x, wg)
        up = jnp.einsum('bsd,hd->bsh', x, wu)
        h = jax.nn.silu(gate) * up
        return jnp.einsum('bsh,dh->bsd', h, wd)
    x = L0_attn_x
    x = _layernorm(x + _L0_attn_ref(x, L0_attn_w_qkv), axis=-1)
    x = _layernorm(x + _L0_ffn_ref(x, L0_ffn_w_gate, L0_ffn_w_up, L0_ffn_w_down), axis=-1)
    return x

_drawn_inputs = setup_inputs


def setup_inputs(seed=0):
    import zlib

    import numpy as np

    out = dict(_drawn_inputs(seed))
    spreads = {}
    factors = {}
    for name, (base, spread) in spreads.items():
        noise = np.random.default_rng([zlib.crc32(name.encode()), seed]).standard_normal(out[name].shape)
        drawn = base * np.exp(spread * noise) if base else spread * noise
        out[name] = jnp.asarray(drawn.astype(out[name].dtype))
    for name, factor in factors.items():
        out[name] = (out[name] * factor).astype(out[name].dtype)
    return out
```

```python
from contextlib import ExitStack

import concourse.bass as bass
from concourse import mybir

F32 = mybir.dt.float32
BF16 = mybir.dt.bfloat16
I32 = mybir.dt.int32
ALU = mybir.AluOpType
ACT = mybir.ActivationFunctionType
AX = mybir.AxisListType

P = 128
B, T, C = 8, 512, 128
H, D = 16, 8
HID = 384
NB = T // P
HG = 4
NG = H // HG
SLOTS = 5
UNITS = 2 * SLOTS
PARTS = 3
TERMS = PARTS * PARTS
KQ = TERMS * D
KS = KQ + PARTS
LAG = 2
VW = 32
MASKED = -3.0e38
SM_SCALE = 1.0 / float(D) ** 0.5
W_SCALE = 1.0 / 127.0
EPS = 1e-5
HC = HID // P


def key_block_place(h, j):
    return ((h, 0), (HG + h, 0), (2 * HG + h // 2, 256 * (h % 2)), (HG + h, 384))[j]


def query_block_place(h, i):
    return ((HG + h, 384), (2 * HG + h // 2, 256 * (h % 2)), (HG + h, 0), (h, 0))[i]


def attention_ffn(nc, x, w_qkv, w_gate, w_up, w_down, out):
    ctx = ExitStack()
    with ctx:
        def sb(name, shape, dt):
            return ctx.enter_context(nc.sbuf_tensor(name, shape, dt))

        def sem(name):
            return ctx.enter_context(nc.semaphore(name))

        psum = ctx.enter_context(nc.psum_tensor("psum", [P, 8, 512], F32))
        st_ps = [psum[:, 0:2, :], psum[:, 2:4, :]]
        mx_ps = [psum[:, 4, :], psum[:, 5, :]]
        pv_ps = psum[:, 6, :]
        misc = psum[:, 7, :]

        identf = sb("identf", [P, P], F32)
        identb = sb("identb", [P, P], BF16)
        maskb = sb("maskb", [P, P], BF16)
        wqkv = sb("wqkv", [P, 3 * C], F32)
        wraw = sb("wraw", [P, 3, HID], I32)
        wdeq = sb("wdeq", [P, 3, HID], F32)
        wT = sb("wT", [P, 3, HID], F32)
        xa = sb("xa", [P, NB, C], F32)
        xT = sb("xT", [P, T], F32)
        res = sb("res", [P, B * NB, C], F32)
        r1 = sb("r1", [P, T], F32)
        parts = sb("parts", [P, 2, PARTS, T], BF16)
        qx = [sb(f"qx{u}", [P, H, T], BF16) for u in range(2)]
        kx = [sb(f"kx{u}", [P, H, T], BF16) for u in range(2)]
        vx = [sb(f"vx{u}", [P, NB, H, VW], F32) for u in range(2)]
        negmax = [sb(f"negmax{u}", [P, HG, NB], F32) for u in range(2)]
        nm_rest = [sb(f"nm_rest{u}", [P, HG * NB], F32) for u in range(2)]
        nm_parts = sb("nm_parts", [P, P // (HG * NB), HG * NB], BF16)
        nm_T = sb("nm_T", [PARTS * HG * NB, P], BF16)
        pt = [sb(f"pt{u}", [P, UNITS, 512], F32) for u in range(2)]
        oT = sb("oT", [P, T], F32)
        rsum = sb("rsum", [P, NB * HG], F32)
        attn = sb("attn", [P, NB, H, D], F32)
        scr_q = nc.dram_tensor("scr_q", (H * D, TERMS, T), BF16, kind="Internal").ap()
        scr_k = nc.dram_tensor("scr_k", (H * D, TERMS, T), BF16, kind="Internal").ap()
        stats = sb("stats", [P, 2, NB, 6], F32)
        mv = sb("mv", [P, 2, NB, 2], F32)
        veps = sb("veps", [P, 2, NB], F32)
        rstd = sb("rstd", [P, 2, NB], F32)
        minus_half = sb("minus_half", [P, NB], F32)
        x1 = [sb(f"x1_{u}", [P, NB, C], F32) for u in range(2)]
        x1T = [sb(f"x1T{u}", [P, T], F32) for u in range(2)]
        sg = [sb(f"sg{u}", [P, T], F32) for u in range(2)]
        hid = sb("hid", [P, HC, T], F32)
        r2 = sb("r2", [P, NB, C], F32)
        yo = [sb(f"yo{u}", [P, NB, C], F32) for u in range(2)]

        x_in = sem("x_in")
        res_in = sem("res_in")
        w_in = sem("w_in")
        wff_in = sem("wff_in")
        const_made = sem("const_made")
        zeroed = sem("zeroed")
        v_zeroed = sem("v_zeroed")
        pool_gate = sem("pool_gate")
        dve_gate = sem("dve_gate")
        ones_made = sem("ones_made")
        xt_made = sem("xt_made")
        q_made = sem("q_made")
        k_made = sem("k_made")
        v_made = sem("v_made")
        nm_turned = sem("nm_turned")
        o_turned = sem("o_turned")
        xt_copied = sem("xt_copied")
        hi_made = sem("hi_made")
        rest_made = sem("rest_made")
        mid_made = sem("mid_made")
        lo_made = sem("lo_made")
        scr_written = sem("scr_written")
        qk_loaded = [[sem(f"qk_loaded{u}{g}") for g in range(NG)] for u in range(2)]
        v_copied = sem("v_copied")
        mx_full = sem("mx_full")
        mx_reduced = sem("mx_reduced")
        nm_hi = sem("nm_hi")
        nm_rst = sem("nm_rst")
        nm_mid = sem("nm_mid")
        nm_split = sem("nm_split")
        nm_copied = sem("nm_copied")
        nm_loaded = sem("nm_loaded")
        st_full = sem("st_full")
        exp_done = sem("exp_done")
        diag_done = sem("diag_done")
        pv_done = sem("pv_done")
        attn_made = sem("attn_made")
        res_made = sem("res_made")
        out_stored = [sem(f"out_stored{u}") for u in range(2)]
        ot_copied = sem("ot_copied")
        rs_made = sem("rs_made")
        wff_deq = sem("wff_deq")
        wff_turned = sem("wff_turned")
        wff_copied = sem("wff_copied")
        st1_made = sem("st1_made")
        mv1_made = sem("mv1_made")
        ve1_made = sem("ve1_made")
        rstd1_made = sem("rstd1_made")
        x1_made = sem("x1_made")
        x1_turned = sem("x1_turned")
        x1t_copied = sem("x1t_copied")
        gate_full = sem("gate_full")
        up_full = sem("up_full")
        silu_done = sem("silu_done")
        hid_made = sem("hid_made")
        y_full = sem("y_full")
        r2_made = sem("r2_made")
        st2_made = sem("st2_made")
        mv2_made = sem("mv2_made")
        ve2_made = sem("ve2_made")
        rstd2_made = sem("rstd2_made")
        yo_made = sem("yo_made")

        x_v = x.rearrange("b (n p) c -> b p n c", p=P)
        out_v = out.rearrange("b (n p) c -> b p n c", p=P)

        def bodies(eng, body):
            with eng.Fori(0, (B - 2) // 2) as i:
                for u in range(2):
                    body(i, u, True, True)
            body((B - 2) // 2, 0, False, True)
            body((B - 2) // 2, 1, False, False)

        def fills(i, u, n):
            return i + (u + n // NG) // 2 + 1, (u + n // NG) % 2

        def whole_batches(eng, step):
            step(0, 0, True, False)
            with eng.Fori(0, (B - 2) // 2) as i:
                step(2 * i + 1, 1, False, False)
                step(2 * i + 2, 0, False, False)
            step(B - 1, 1, False, True)

        block = ctx.enter_context(nc.Block())

        @block.sync
        def _(sp):
            def load_x(b):
                sp.dma_start(xa[:], x_v[bass.ds(b, 1)].rearrange("a p n c -> (a p) n c")).then_inc(x_in, 16)

            def write_parts(b):
                sp.wait_ge(lo_made, 2 * b + 1)
                for t in range(PARTS):
                    sp.dma_start(scr_q[:, t::PARTS, :], parts[:, 0]).then_inc(scr_written, 16)
                sp.wait_ge(lo_made, 2 * b + 2)
                for t in range(PARTS):
                    sp.dma_start(scr_k[:, PARTS * t:PARTS * t + PARTS, :], parts[:, 1]).then_inc(scr_written, 16)

            def read_rows(b, u):
                sp.wait_ge(scr_written, 16 * 2 * PARTS * b + 16 * 2 * PARTS)
                for g in range(NG):
                    for dst, scr in ((qx[u], scr_q), (kx[u], scr_k)):
                        src = scr[g * HG * D:(g + 1) * HG * D].rearrange("(h d) e t -> (d e) h t", h=HG)
                        sp.dma_start(dst[0:KQ, g * HG:(g + 1) * HG, :], src).then_inc(qk_loaded[u][g], 16)

            def load_negmax(m, u, g):
                sp.wait_ge(nm_copied, m + 1)
                for t in range(PARTS):
                    dst = qx[u][KQ + t:KQ + t + 1, g * HG:(g + 1) * HG, :]
                    sp.dma_start(dst.rearrange("p h (i q) -> p (h i) q", i=NB),
                                 nm_T[t * HG * NB:(t + 1) * HG * NB, :]).then_inc(nm_loaded, 16)

            for u in range(2):
                sp.sem_inc(out_stored[u], 16)
            load_x(0)
            sp.dma_start(wqkv[:], w_qkv).then_inc(w_in, 16)
            sp.wait_ge(xt_made, 1)
            load_x(1)
            sp.wait_ge(ones_made, 2)
            write_parts(0)
            read_rows(0, 0)
            sp.dma_start(res[:], x.rearrange("b (n p) c -> p (b n) c", p=P)).then_inc(res_in, 16)
            for n, w in enumerate((w_gate, w_up)):
                sp.dma_start(wraw[:, n, :].rearrange("p (c d) -> p c d", c=HC),
                             w.rearrange("(c p) d -> p c d", p=P)).then_inc(wff_in, 16)
            sp.dma_start(wraw[:, 2, :], w_down).then_inc(wff_in, 16)
            for g in range(NG):
                sp.wait_ge(qk_loaded[0][g], 32)
            write_parts(1)
            read_rows(1, 1)
            load_negmax(0, 0, 0)
            load_negmax(1, 0, 1)

            def body(i, u, prep, more):
                b = 2 * i + u
                if prep:
                    sp.wait_ge(xt_made, b + 2)
                    load_x(b + 2)
                for n in range(NG):
                    if more or n + 2 < NG:
                        load_negmax(NG * b + n + 2, fills(i, u, n + 2)[1], (n + 2) % NG)
                    if n == 2 and prep:
                        for g in range(NG):
                            sp.wait_ge(qk_loaded[1 - u][g], 32 * fills(i, u, NG)[0])
                        write_parts(b + 2)
                if prep:
                    sp.wait_ge(st_full, SLOTS * NG * b + SLOTS * NG)
                    read_rows(b + 2, u)

            bodies(sp, body)

            with sp.Fori(0, B // 2) as i:
                for u in range(2):
                    sp.wait_ge(yo_made, NB * 2 * i + NB * (u + 1))
                    sp.dma_start(out_v[bass.ds(2 * i + u, 1)].rearrange("a p n c -> (a p) n c"),
                                 yo[u][:]).then_inc(out_stored[u], 16)
            for u in range(2):
                sp.wait_ge(out_stored[u], 16 + 16 * (B // 2))

        @block.tensor
        def _(pe):
            free = [None]

            def take_misc(then):
                if free[0] is not None:
                    pe.wait_ge(*free[0])
                free[0] = then

            def transposes4(dst, src):
                for n in range(NB):
                    last = pe.transpose(dst[:, P * n:P * n + P], src[:, P * n:P * n + P], identf[:])
                return last

            def turn_x(b):
                pe.wait_ge(x_in, 16 * b + 16)
                take_misc((xt_copied, b + 1))
                transposes4(misc, xa[:].rearrange("p n c -> p (n c)")).then_inc(xt_made, 1)

            def project_qk(b, n):
                pe.wait_ge(xt_copied, b + 1)
                take_misc((rest_made, 2 * b + n + 1))
                pe.matmul(misc, wqkv[:, C * n:C * n + C], xT[:], start=True, stop=True).then_inc((q_made, k_made)[n], 1)

            def project_v(b):
                pe.wait_ge(xt_copied, b + 1)
                take_misc((v_copied, b + 1))
                for n in range(NB):
                    last = pe.matmul(misc[:, C * n:C * n + C], xT[:, P * n:P * n + P], wqkv[:, 2 * C:3 * C],
                                     start=True, stop=True)
                last.then_inc(v_made, 1)

            def turn_negmax(m):
                pe.wait_ge(nm_split, m + 1)
                take_misc((nm_copied, m + 1))
                pe.transpose(misc[:, 0:P // 2].bitcast(BF16),
                             nm_parts[:].rearrange("p t c -> p (t c)"), identb[:]).then_inc(nm_turned, 1)

            def turn_out(G):
                pe.wait_ge(ot_copied, G + 1)
                take_misc((attn_made, G + 2))
                transposes4(misc, oT[:]).then_inc(o_turned, 1)

            def score_slot(G, u, g, s):
                if s == 0:
                    pe.wait_ge(nm_loaded, 16 * PARTS * G + 16 * PARTS)
                if not (isinstance(G, int) and G == 0 and s < 2):
                    pe.wait_ge(exp_done, SLOTS * G + s - 1)
                for bank in (2 * s, 2 * s + 1):
                    blocks = [(h, j) for h in range(HG) for j in range(NB) if key_block_place(h, j)[0] == bank]
                    for n, (h, j) in enumerate(blocks):
                        col, width = key_block_place(h, j)[1], T - P * j
                        last = pe.matmul(st_ps[(g * SLOTS + s) % 2][:, bank % 2, col:col + width],
                                         kx[u][0:KS, HG * g + h, P * j:P * j + P],
                                         qx[u][0:KS, HG * g + h, P * j:T], start=(n == 0),
                                         stop=(n == len(blocks) - 1), skip_group_check=True)
                last.then_inc(st_full, 1)

            def max_bank(M, u, g, filled, bank):
                if bank == 0:
                    pe.wait_ge(qk_loaded[u][g], 32 * filled)
                if not (isinstance(M, int) and M == 0 and bank < 2):
                    pe.wait_ge(mx_reduced, UNITS * M + bank - 1)
                dst = mx_ps[bank % 2]
                blocks = [(h, i) for h in range(HG) for i in range(NB) if query_block_place(h, i)[0] == bank]
                for n, (h, i) in enumerate(blocks):
                    col, width = query_block_place(h, i)[1], P * (i + 1)
                    pe.matmul(dst[:, col:col + width], qx[u][0:KQ, HG * g + h, P * i:P * i + P],
                              kx[u][0:KQ, HG * g + h, 0:width], start=(n == 0), stop=False, skip_group_check=True)
                    last = pe.matmul(dst[:, col + width - P:col + width], identb[:], maskb[:],
                                     start=False, stop=(n == len(blocks) - 1), skip_group_check=True)
                last.then_inc(mx_full, 1)

            def values(G, b, u, g, j):
                if j == 0:
                    pe.wait_ge(v_copied, b + 1)
                    if not (isinstance(G, int) and G == 0):
                        pe.wait_ge(ot_copied, G)
                pe.wait_ge(diag_done, NB * G + (1, 2, 4, 3)[j])
                if j == 0:
                    pe.wait_ge(exp_done, SLOTS * G + SLOTS)
                for h in range(HG):
                    bank, col = key_block_place(h, j)
                    last = pe.matmul(pv_ps[VW * h:VW * h + VW, P * j:T], vx[u][:, j, HG * g + h, :],
                                     pt[g % 2][:, bank, col:col + T - P * j], start=(j == 0), stop=(j == NB - 1),
                                     skip_group_check=True)
                if j == NB - 1:
                    last.then_inc(pv_done, 1)

            pe.sem_inc(pv_done, 1)
            pe.wait_ge(const_made, 3)
            turn_x(0)
            pe.wait_ge(w_in, 16)
            project_qk(0, 0)
            project_qk(0, 1)
            project_v(0)
            turn_x(1)
            project_qk(1, 0)
            project_qk(1, 1)
            for M in range(LAG):
                for bank in range(UNITS):
                    max_bank(M, 0, M, 1, bank)
                if M == 0:
                    turn_negmax(0)
            for s in range(SLOTS):
                score_slot(0, 0, 0, s)
                for bank in (2 * s, 2 * s + 1):
                    max_bank(LAG, 0, LAG, 1, bank)
                if s == 1:
                    turn_negmax(1)
            free[0] = None

            def body(i, u, prep, more):
                b = 2 * i + u
                for n in range(NG if more else NG - 1):
                    G = NG * b + n + 1
                    for s in range(SLOTS):
                        score_slot(G, fills(i, u, n + 1)[1], (n + 1) % NG, s)
                        if more or n + 1 + LAG < NG:
                            filled, um = fills(i, u, n + 1 + LAG)
                            for bank in (2 * s, 2 * s + 1):
                                max_bank(G + LAG, um, (n + 1 + LAG) % NG, filled, bank)
                        if s < NB:
                            values(G - 1, b, u, n, s)
                        if s == 0 and n == 2 and prep:
                            project_qk(b + 2, 0)
                        if s == 1 and (more or n + 2 < NG):
                            if n == 0:
                                pe.wait_ge(nm_copied, G + 1)
                                pe.wait_ge(attn_made, NG * b + 1)
                            turn_negmax(G + 1)
                        if s == 2:
                            if n == 0 and more:
                                project_v(b + 1)
                            if n == 1 and prep:
                                turn_x(b + 2)
                            if n == 2 and prep:
                                project_qk(b + 2, 1)
                        if s == SLOTS - 1:
                            turn_out(G - 1)
                free[0] = None

            bodies(pe, body)
            for j in range(NB):
                values(NG * B - 1, B - 1, 1, NG - 1, j)
            pe.wait_ge(attn_made, NG * B)
            turn_out(NG * B - 1)

            pe.wait_ge(wff_deq, 3)
            for n in range(3):
                take_misc((wff_copied, n + 1))
                for c in range(HC):
                    last = pe.transpose(misc[:, P * c:P * c + P], wdeq[:, n, P * c:P * c + P], identf[:])
                last.then_inc(wff_turned, 1)

            def turn_x1(c, u):
                pe.wait_ge(x1_made, NB * c + NB)
                if not (isinstance(c, int) and c == 0):
                    pe.wait_ge(x1t_copied, c)
                transposes4(psum[:, 0, :], x1[u][:].rearrange("p n c -> p (n c)")).then_inc(x1_turned, 1)

            def ffn(c, u, first, last_one):
                pe.wait_ge(x1t_copied, c + 1)
                for m in range(HC):
                    k = HC * u + m
                    if not (first and m < 2):
                        pe.wait_ge(silu_done, HC * c + m - 1)
                        pe.wait_ge(hid_made, HC * c + m - 1)
                    pe.matmul(psum[:, 1 + k % 2, :], wT[:, 0, P * m:P * m + P], x1T[u][:],
                              start=True, stop=True).then_inc(gate_full, 1)
                    pe.matmul(psum[:, 3 + k % 2, :], wT[:, 1, P * m:P * m + P], x1T[u][:],
                              start=True, stop=True).then_inc(up_full, 1)
                if not last_one:
                    turn_x1(c + 1, 1 - u)
                if not first:
                    pe.wait_ge(r2_made, c)
                pe.wait_ge(hid_made, HC * c + HC)
                for n in range(NB):
                    for m in range(HC):
                        last = pe.matmul(psum[:, 5, C * n:C * n + C], hid[:, m, P * n:P * n + P],
                                         wT[:, 2, P * m:P * m + P], start=(m == 0), stop=(m == HC - 1))
                last.then_inc(y_full, 1)

            pe.wait_ge(wff_copied, 3)
            turn_x1(0, 0)
            whole_batches(pe, ffn)

        @block.scalar
        def _(act):
            copy = ACT.Copy

            def copy_xt(b):
                act.wait_ge(xt_made, b + 1)
                if not (isinstance(b, int) and b == 0):
                    act.wait_ge(k_made, b)
                    act.wait_ge(v_made, b)
                act.activation(xT[:], misc, copy).then_inc(xt_copied, 1)

            def first_part(b, n):
                act.wait_ge((q_made, k_made)[n], b + 1)
                if not (isinstance(b, int) and b == 0):
                    act.wait_ge(scr_written, 16 * 2 * PARTS * b)
                act.activation(parts[:, n, 0, :], misc, copy).then_inc(hi_made, 1)

            def copy_v(b, u):
                act.wait_ge(v_made, b + 1)
                if not (isinstance(b, int) and b < 2):
                    act.wait_ge(pv_done, NG * b - NG + 1)
                act.activation(vx[u][:, :, :, 0:D], misc.rearrange("p (n h d) -> p n h d", n=NB, h=H),
                               copy).then_inc(v_copied, 1)

            def exp_slot(G, g, s):
                act.wait_ge(st_full, SLOTS * G + s + 1)
                if s == 0 and not (isinstance(G, int) and G < 2):
                    act.wait_ge(pv_done, G)
                act.activation(pt[g % 2][:, 2 * s:2 * s + 2, :], st_ps[(g * SLOTS + s) % 2], ACT.Exp,
                               scale=SM_SCALE).then_inc(exp_done, 1)

            def copy_negmax(m):
                act.wait_ge(nm_turned, m + 1)
                if not (isinstance(m, int) and m == 0):
                    act.wait_ge(nm_loaded, 16 * PARTS * m)
                act.activation(nm_T[:], misc[0:PARTS * HG * NB, 0:P // 2].bitcast(BF16), copy).then_inc(nm_copied, 1)

            def copy_out(G):
                act.wait_ge(pv_done, G + 2)
                if not (isinstance(G, int) and G == 0):
                    act.wait_ge(o_turned, G)
                act.activation(oT[:], pv_ps, copy).then_inc(ot_copied, 1)

            copy_xt(0)
            first_part(0, 0)
            first_part(0, 1)
            act.wait_ge(ones_made, 4)
            copy_v(0, 0)
            copy_xt(1)
            first_part(1, 0)
            first_part(1, 1)
            copy_negmax(0)
            for s in range(SLOTS):
                exp_slot(0, 0, s)
                if s == 1:
                    copy_negmax(1)

            def body(i, u, prep, more):
                b = 2 * i + u
                for n in range(NG if more else NG - 1):
                    G = NG * b + n + 1
                    for s in range(SLOTS):
                        exp_slot(G, (n + 1) % NG, s)
                        if s == 0 and n == 2 and prep:
                            first_part(b + 2, 0)
                        if s == 1 and (more or n + 2 < NG):
                            copy_negmax(G + 1)
                        if s == 2:
                            if n == 0 and more:
                                copy_v(b + 1, 1 - u)
                            if n == 1 and prep:
                                copy_xt(b + 2)
                            if n == 2 and prep:
                                first_part(b + 2, 1)
                        if s == 3:
                            copy_out(G - 1)

            bodies(act, body)
            copy_out(NG * B - 1)

            for n in range(3):
                act.wait_ge(wff_turned, n + 1)
                act.activation(wT[:, n, :], misc[:, 0:HID], copy).then_inc(wff_copied, 1)

            def copy_x1t(c, u):
                act.wait_ge(x1_turned, c + 1)
                if not (isinstance(c, int) and c < 2):
                    act.wait_ge(up_full, HC * c - HC)
                act.activation(x1T[u][:], psum[:, 0, :], copy).then_inc(x1t_copied, 1)

            def ffn(c, u, first, last_one):
                for m in range(HC):
                    k = HC * u + m
                    act.wait_ge(gate_full, HC * c + m + 1)
                    if not (first and m < 2):
                        act.wait_ge(hid_made, HC * c + m - 1)
                    act.activation(sg[k % 2][:], psum[:, 1 + k % 2, :], ACT.Silu).then_inc(silu_done, 1)
                if not last_one:
                    copy_x1t(c + 1, 1 - u)

            copy_x1t(0, 0)
            whole_batches(act, ffn)

        @block.vector
        def _(dve):
            def rest(b, n):
                dve.wait_ge(hi_made, 2 * b + n + 1)
                if not (isinstance(b, int) and b == 0 and n == 0):
                    dve.wait_ge(lo_made, 2 * b + n)
                dve.tensor_tensor(r1[:], misc, parts[:, n, 0, :], ALU.subtract).then_inc(rest_made, 1)

            def reduce_bank(M, g, bank):
                if bank == 0 and not (isinstance(M, int) and M < 2):
                    dve.wait_ge(nm_split, M - 1)
                dve.wait_ge(mx_full, UNITS * M + bank + 1)
                src, nm = mx_ps[bank % 2], negmax[g % 2]
                if bank < HG:
                    last = dve.tensor_reduce(nm[:, bank, 3:4], src, AX.X, ALU.max, negate=True)
                elif bank < 2 * HG:
                    dve.tensor_reduce(nm[:, bank - HG, 2:3], src[:, 0:384], AX.X, ALU.max, negate=True)
                    last = dve.tensor_reduce(nm[:, bank - HG, 0:1], src[:, 384:512], AX.X, ALU.max, negate=True)
                else:
                    h = 2 * (bank - 2 * HG)
                    last = dve.tensor_reduce(nm[:, h:h + 2, 1], src.rearrange("p (h k) -> p h k", h=2), AX.X, ALU.max,
                                             negate=True)
                last.then_inc(mx_reduced, 1)

            def normalise(G, g):
                dve.wait_ge(o_turned, G + 1)
                turned = misc.rearrange("p (r w) -> p r w", w=VW)
                dve.reciprocal(rsum[:], turned[:, :, D]).then_inc(rs_made, 1)
                if g == 0 and not (isinstance(G, int) and G == 0):
                    dve.wait_ge(res_made, res_count(G) + 1)
                dve.wait_ge(rs_made, G + 1)
                dve.tensor_tensor(attn[:, :, HG * g:HG * g + HG, :],
                                  misc.rearrange("p (n h w) -> p n h w", n=NB, h=HG)[:, :, :, 0:D],
                                  rsum[:].rearrange("p (n h) -> p n h", n=NB).unsqueeze(3)
                                  .to_broadcast([P, NB, HG, D]), ALU.mult).then_inc(attn_made, 1)

            batch = [0]

            def res_count(G):
                return batch[0]

            dve.sem_inc(attn_made, 1)
            for t in kx:
                dve.memset(t[64:96, :, :], 1.0).then_inc(ones_made, 1)
            for u in range(2):
                dve.wait_ge(v_zeroed, 2)
                dve.memset(vx[u][:, :, :, D:D + 1], 1.0).then_inc(ones_made, 1)
            for b in range(2):
                for n in range(2):
                    rest(b, n)
            for M in range(LAG):
                for bank in range(UNITS):
                    reduce_bank(M, M, bank)
            for bank in range(UNITS):
                reduce_bank(LAG, LAG, bank)

            def body(i, u, prep, more):
                b = 2 * i + u
                batch[0] = b
                for n in range(NG if more else NG - 1):
                    G = NG * b + n + 1
                    for s in range(SLOTS):
                        if more or n + 1 + LAG < NG:
                            for bank in (2 * s, 2 * s + 1):
                                reduce_bank(G + LAG, (n + 1 + LAG) % NG, bank)
                        if n == 2 and prep and s in (0, 2):
                            rest(b + 2, s // 2)
                    normalise(G - 1, n)

            bodies(dve, body)
            normalise(NG * B - 1, NG - 1)

            def norm_stats(src, k, st_made, mv_made, count):
                for n in range(NB):
                    dve.bn_stats(stats[:, k, n, :], src(n)).then_inc(st_made, 1)
                dve.wait_ge(st_made, count)
                dve.sem_inc(dve_gate, 1)
                for n in range(NB):
                    dve.bn_aggr(mv[:, k, n, :], stats[:, k, n, :]).then_inc(mv_made, 1)

            def stats1(c):
                dve.wait_ge(res_made, c + 2)
                if not (isinstance(c, int) and c == 0):
                    dve.wait_ge(ve1_made, c)
                    dve.wait_ge(x1_made, NB * c)
                norm_stats(lambda n: res[:, bass.ds(NB * c + n, 1), :].rearrange("p a c -> p (a c)"), 0, st1_made,
                           mv1_made, NB * c + NB)

            def norm1(c, u):
                dve.wait_ge(rstd1_made, c + 1)
                if not (isinstance(c, int) and c < 2):
                    dve.wait_ge(x1_turned, c - 1)
                    dve.wait_ge(r2_made, c - 1)
                for n in range(NB):
                    dve.tensor_scalar(x1[u][:, n, :], res[:, bass.ds(NB * c + n, 1), :].rearrange("p a c -> p (a c)"),
                                      mv[:, 0, n, 0:1], rstd[:, 0, n:n + 1], ALU.subtract, ALU.mult).then_inc(x1_made, 1)

            def norm2(c, u):
                dve.wait_ge(rstd2_made, c + 1)
                if not (isinstance(c, int) and c < 2):
                    dve.wait_ge(out_stored[u], 8 * (c - u) + 16)
                for n in range(NB):
                    dve.tensor_scalar(yo[u][:, n, :], r2[:, n, :], mv[:, 1, n, 0:1], rstd[:, 1, n:n + 1],
                                      ALU.subtract, ALU.mult).then_inc(yo_made, 1)

            def ffn(c, u, first, last_one):
                if not last_one:
                    stats1(c + 1)
                if not first:
                    norm2(c - 1, 1 - u)
                for m in range(HC):
                    k = HC * u + m
                    dve.wait_ge(silu_done, HC * c + m + 1)
                    dve.wait_ge(up_full, HC * c + m + 1)
                    if not first and m == 0:
                        dve.wait_ge(y_full, c)
                    dve.tensor_tensor(hid[:, m, :], psum[:, 3 + k % 2, :], sg[k % 2][:], ALU.mult).then_inc(hid_made, 1)
                    if m == 0 and not last_one:
                        norm1(c + 1, 1 - u)
                dve.wait_ge(y_full, c + 1)
                if not first:
                    dve.wait_ge(yo_made, NB * c)
                dve.tensor_tensor(r2[:].rearrange("p n c -> p (n c)"), psum[:, 5, :],
                                  x1[u][:].rearrange("p n c -> p (n c)"), ALU.add).then_inc(r2_made, 1)
                dve.wait_ge(r2_made, c + 1)
                norm_stats(lambda n: r2[:, n, :], 1, st2_made, mv2_made, NB * c + NB)

            stats1(0)
            norm1(0, 0)
            whole_batches(dve, ffn)
            norm2(B - 1, 1)

        @block.gpsimd
        def _(pool):
            pool.sem_inc(res_made, 1)
            pool.memset(identf[:], 0.0).then_inc(zeroed, 1)
            pool.memset(maskb[:], 0.0).then_inc(zeroed, 1)
            pool.wait_ge(zeroed, 2)
            pool.affine_select(out=identf[:], in_=identf[:], pattern=[[-1, P]], compare_op=ALU.not_equal, fill=1.0,
                               base=0, channel_multiplier=1).then_inc(const_made, 1)
            pool.affine_select(out=maskb[:], in_=maskb[:], pattern=[[-1, P]], compare_op=ALU.is_ge, fill=MASKED,
                               base=0, channel_multiplier=1).then_inc(const_made, 1)
            pool.wait_ge(const_made, 1)
            pool.tensor_scalar(identb[:], identf[:], 1.0, 0.0, ALU.mult, ALU.add).then_inc(const_made, 1)
            for t in vx:
                pool.memset(t[:], 0.0).then_inc(v_zeroed, 1)
            pool.memset(minus_half[:], -0.5).then_inc(v_zeroed, 1)
            pool.memset(nm_parts[:], 0.0).then_inc(v_zeroed, 1)
            pool.wait_ge(v_zeroed, 4)

            def split_qk(b, n):
                pool.wait_ge(rest_made, 2 * b + n + 1)
                pool.sem_inc(pool_gate, 1)
                pool.tensor_scalar(parts[:, n, 1, :], r1[:], 1.0, 0.0, ALU.mult, ALU.add).then_inc(mid_made, 1)
                pool.wait_ge(mid_made, 2 * b + n + 1)
                pool.tensor_tensor(parts[:, n, 2, :], r1[:], parts[:, n, 1, :], ALU.subtract).then_inc(lo_made, 1)

            def split_negmax(M, g):
                nm = negmax[g % 2][:].rearrange("p h i -> p (h i)")
                pool.wait_ge(mx_reduced, UNITS * M + UNITS)
                if not (isinstance(M, int) and M == 0):
                    pool.wait_ge(nm_turned, M)
                pool.sem_inc(pool_gate, 1)
                pool.tensor_scalar(nm_parts[:, 0, :], nm, 1.0, 0.0, ALU.mult, ALU.add).then_inc(nm_hi, 1)
                pool.wait_ge(nm_hi, M + 1)
                pool.tensor_tensor(nm_rest[g % 2][:], nm, nm_parts[:, 0, :], ALU.subtract).then_inc(nm_rst, 1)
                pool.wait_ge(nm_rst, M + 1)
                pool.sem_inc(pool_gate, 1)
                pool.tensor_scalar(nm_parts[:, 1, :], nm_rest[g % 2][:], 1.0, 0.0, ALU.mult, ALU.add).then_inc(nm_mid, 1)
                pool.wait_ge(nm_mid, M + 1)
                pool.tensor_tensor(nm_parts[:, 2, :], nm_rest[g % 2][:], nm_parts[:, 1, :],
                                   ALU.subtract).then_inc(nm_split, 1)

            def clear_diagonal(G, g, s):
                for j in {1: (0,), 3: (1, 3), 4: (2,)}[s]:
                    bank, col = key_block_place(0, j)
                    step = 256 if j == 2 else 512
                    blocks = (pt[g % 2][:].rearrange("p b q -> p (b q)")[:, 512 * bank:512 * bank + HG * step]
                              .rearrange("p (h q) -> p h q", h=HG)[:, :, col:col + P])
                    pool.wait_ge(exp_done, SLOTS * G + s + 1)
                    pool.sem_inc(pool_gate, 1)
                    pool.affine_select(out=blocks, in_=blocks, pattern=[[0, HG], [1, P]], compare_op=ALU.is_ge,
                                       fill=0.0, base=0, channel_multiplier=-1).then_inc(diag_done, 1)

            def add_attention(b):
                if isinstance(b, int) and b == 0:
                    pool.wait_ge(res_in, 16)
                pool.wait_ge(attn_made, NG * b + NG + 1)
                x_b = res[:, bass.ds(NB * b, NB), :]
                pool.tensor_tensor(x_b, x_b, attn[:].rearrange("p n h d -> p n (h d)"), ALU.add).then_inc(res_made, 1)

            for b in range(2):
                for n in range(2):
                    split_qk(b, n)
            split_negmax(0, 0)
            split_negmax(1, 1)
            pool.wait_ge(res_in, 16)
            clear_diagonal(0, 0, 1)
            clear_diagonal(0, 0, 3)
            clear_diagonal(0, 0, 4)
            split_negmax(2, 0)

            def body(i, u, prep, more):
                b = 2 * i + u
                for n in range(NG if more else NG - 1):
                    G = NG * b + n + 1
                    if n == 2 and prep:
                        split_qk(b + 2, 0)
                    clear_diagonal(G, (n + 1) % NG, 1)
                    clear_diagonal(G, (n + 1) % NG, 3)
                    if n == 2 and prep:
                        split_qk(b + 2, 1)
                    clear_diagonal(G, (n + 1) % NG, 4)
                    if more or n + 1 + LAG < NG:
                        split_negmax(G + LAG, (n + 1 + LAG) % NG)
                if more:
                    add_attention(b)

            bodies(pool, body)
            add_attention(B - 1)

            pool.wait_ge(wff_in, 48)
            for n in range(3):
                pool.tensor_scalar(wdeq[:, n, :], wraw[:, n, :], W_SCALE, 0.0, ALU.mult, ALU.add).then_inc(wff_deq, 1)

            def inverse_deviation(c, k, mv_made, ve_made, rstd_made):
                pool.wait_ge(mv_made, NB * c + NB)
                pool.sem_inc(pool_gate, 1)
                pool.tensor_scalar(veps[:, k, :], mv[:, k, :, 1], 1.0, EPS, ALU.mult, ALU.add).then_inc(ve_made, 1)
                pool.wait_ge(ve_made, c + 1)
                pool.tensor_tensor(rstd[:, k, :], veps[:, k, :], minus_half[:], ALU.pow).then_inc(rstd_made, 1)

            def ffn(c, u, first, last_one):
                if not last_one:
                    inverse_deviation(c + 1, 0, mv1_made, ve1_made, rstd1_made)
                inverse_deviation(c, 1, mv2_made, ve2_made, rstd2_made)

            inverse_deviation(0, 0, mv1_made, ve1_made, rstd1_made)
            whole_batches(pool, ffn)


_INS = ["L0_attn_x", "L0_attn_w_qkv", "L0_ffn_w_gate", "L0_ffn_w_up", "L0_ffn_w_down"]


def kernel(**inputs):
    import numpy as np
    import concourse.bacc as bacc
    from concourse.bass_utils import run_bass_kernel_spmd

    nc = bacc.Bacc("TRN2", target_bir_lowering=False, num_devices=1)
    arrays, args = {}, []
    for name in _INS:
        a = np.ascontiguousarray(inputs[name])
        arrays[name] = a
        args.append(nc.dram_tensor(name, a.shape, mybir.dt.from_np(a.dtype), kind="ExternalInput").ap())
    out = nc.dram_tensor("out", (B, T, C), F32, kind="ExternalOutput").ap()
    attention_ffn(nc, *args, out)
    return run_bass_kernel_spmd(nc, [arrays], core_ids=[0]).results[0]["out"]
```

```python
from contextlib import ExitStack

import concourse.bass as bass
from concourse import mybir

F32 = mybir.dt.float32
BF16 = mybir.dt.bfloat16
I32 = mybir.dt.int32
ALU = mybir.AluOpType
ACT = mybir.ActivationFunctionType
AX = mybir.AxisListType

P = 128
B, T, C = 8, 512, 128
H, D = 16, 8
HID = 384
NB = T // P
HG = 4
NG = H // HG
SLOTS = 5
UNITS = 2 * SLOTS
QG = T // 64
MX_BANKS = 9
PARTS = 3
TERMS = PARTS * PARTS
KQ = TERMS * D
BF16_ONES = (1 + 127 / 2 ** 16)
KZ = 96
KS = KZ + PARTS
NM_DMAS = 16 * PARTS * 2
LAG = 2
VW = 32
MASKED = -3.0e38
SM_SCALE = 1.0 / float(D) ** 0.5
W_SCALE = 1.0 / 127.0
EPS = 1e-5
HC = HID // P


def key_block_place(h, j):
    return ((h, 0), (HG + h, 0), (2 * HG + h // 2, 256 * (h % 2)), (HG + h, 384))[j]


def max_segments(bank):
    pair, n = bank // 4, bank % 4
    if bank == 2 * 4:
        return [(0, 3, 0), (1, 3, 256)]
    return [(pair, 7 - n, 0)] + ([(pair, n - 1, 64 * (8 - n))] if n else [])


def attention_ffn(nc, x, w_qkv, w_gate, w_up, w_down, out):
    ctx = ExitStack()
    with ctx:
        def sb(name, shape, dt):
            return ctx.enter_context(nc.sbuf_tensor(name, shape, dt))

        def sem(name):
            return ctx.enter_context(nc.semaphore(name))

        psum = ctx.enter_context(nc.psum_tensor("psum", [P, 8, 512], F32))
        st_ps = [psum[:, 0:2, :], psum[:, 2:4, :]]
        mx_ps = [psum[:, 4, :], psum[:, 5, :]]
        pv_ps = psum[:, 6, :]
        misc = psum[:, 7, :]

        identf = sb("identf", [P, P], F32)
        identb = sb("identb", [P, P], BF16)
        mask = sb("mask", [P, T], F32)
        wqkv = sb("wqkv", [P, 3 * C], F32)
        wraw = sb("wraw", [P, 3, HID], I32)
        wdeq = sb("wdeq", [P, 3, HID], F32)
        wT = sb("wT", [P, 3, HID], F32)
        xa = sb("xa", [P, NB, C], F32)
        xT = sb("xT", [P, T], F32)
        res = sb("res", [P, B * NB, C], F32)
        r1 = sb("r1", [P, T], F32)
        parts = sb("parts", [P, 2, PARTS, T], BF16)
        qx = [sb(f"qx{u}", [P, H, T], BF16) for u in range(2)]
        kx = [sb(f"kx{u}", [P, H, T], BF16) for u in range(2)]
        vx = [sb(f"vx{u}", [P, NB, H, VW], F32) for u in range(2)]
        negmax = [sb(f"negmax{u}", [P, HG // 2 * QG], F32) for u in range(2)]
        nm_rest = [sb(f"nm_rest{u}", [P, HG * NB], F32) for u in range(2)]
        nm_parts = sb("nm_parts", [P, P // (HG * NB), HG * NB], BF16)
        nm_T = sb("nm_T", [PARTS * HG * NB, P], BF16)
        pt = [sb(f"pt{u}", [P, UNITS, 512], F32) for u in range(2)]
        oT = sb("oT", [P, T], F32)
        rsum = sb("rsum", [P, NB * HG], F32)
        attn = sb("attn", [P, NB, H, D], F32)
        scr_q = [nc.dram_tensor(f"scr_q{u}", (H * D, TERMS, T), BF16, kind="Internal").ap() for u in range(2)]
        scr_k = [nc.dram_tensor(f"scr_k{u}", (H * D, TERMS, T), BF16, kind="Internal").ap() for u in range(2)]
        stats = sb("stats", [P, 2, NB, 6], F32)
        mv = sb("mv", [P, 2, NB, 2], F32)
        veps = sb("veps", [P, 2, NB], F32)
        rstd = sb("rstd", [P, 2, NB], F32)
        minus_half = sb("minus_half", [P, NB], F32)
        x1 = [sb(f"x1_{u}", [P, NB, C], F32) for u in range(2)]
        x1T = [sb(f"x1T{u}", [P, T], F32) for u in range(2)]
        sg = [sb(f"sg{u}", [P, T], F32) for u in range(2)]
        hid = sb("hid", [P, HC, T], F32)
        r2 = sb("r2", [P, NB, C], F32)
        yo = [sb(f"yo{u}", [P, NB, C], F32) for u in range(2)]

        x_in = sem("x_in")
        res_in = sem("res_in")
        w_in = sem("w_in")
        wff_in = sem("wff_in")
        const_made = sem("const_made")
        zeroed = sem("zeroed")
        v_zeroed = sem("v_zeroed")
        pool_gate = sem("pool_gate")
        dve_gate = sem("dve_gate")
        ones_made = sem("ones_made")
        v_ones = sem("v_ones")
        xt_made = sem("xt_made")
        q_made = sem("q_made")
        k_made = sem("k_made")
        v_made = sem("v_made")
        nm_turned = sem("nm_turned")
        xt_copied = sem("xt_copied")
        hi_made = sem("hi_made")
        rest_made = sem("rest_made")
        mid_made = sem("mid_made")
        lo_made = sem("lo_made")
        scr_written = sem("scr_written")
        qk_loaded = [[sem(f"qk_loaded{u}{g}") for g in range(NG)] for u in range(2)]
        v_copied = sem("v_copied")
        mx_full = sem("mx_full")
        mx_reduced = sem("mx_reduced")
        nm_hi = sem("nm_hi")
        nm_rst = sem("nm_rst")
        nm_mid = sem("nm_mid")
        nm_split = sem("nm_split")
        nm_copied = sem("nm_copied")
        nm_loaded = sem("nm_loaded")
        st_full = sem("st_full")
        exp_done = sem("exp_done")
        diag_done = sem("diag_done")
        pv_done = sem("pv_done")
        attn_made = sem("attn_made")
        res_made = sem("res_made")
        out_stored = [sem(f"out_stored{u}") for u in range(2)]
        ot_copied = sem("ot_copied")
        o_turned = sem("o_turned")
        rs_made = sem("rs_made")
        wff_deq = sem("wff_deq")
        wff_turned = sem("wff_turned")
        wff_copied = sem("wff_copied")
        st1_made = sem("st1_made")
        mv1_made = sem("mv1_made")
        ve1_made = sem("ve1_made")
        rstd1_made = sem("rstd1_made")
        x1_made = sem("x1_made")
        x1_turned = sem("x1_turned")
        x1t_copied = sem("x1t_copied")
        gate_full = sem("gate_full")
        up_full = sem("up_full")
        silu_done = sem("silu_done")
        hid_made = sem("hid_made")
        y_full = sem("y_full")
        r2_made = sem("r2_made")
        st2_made = sem("st2_made")
        mv2_made = sem("mv2_made")
        ve2_made = sem("ve2_made")
        rstd2_made = sem("rstd2_made")
        yo_made = sem("yo_made")

        x_v = x.rearrange("b (n p) c -> b p n c", p=P)
        out_v = out.rearrange("b (n p) c -> b p n c", p=P)

        def bodies(eng, body):
            with eng.Fori(0, (B - 2) // 2) as i:
                for u in range(2):
                    body(i, u, True, True)
            body((B - 2) // 2, 0, False, True)
            body((B - 2) // 2, 1, False, False)

        def fills(i, u, n):
            return i + (u + n // NG) // 2 + 1, (u + n // NG) % 2

        def whole_batches(eng, step):
            step(0, 0, True, False)
            with eng.Fori(0, (B - 4) // 2) as i:
                step(2 * i + 1, 1, False, False)
                step(2 * i + 2, 0, False, False)
            step(B - 3, 1, False, False)
            step(B - 2, 0, False, False)
            step(B - 1, 1, False, True)

        block = ctx.enter_context(nc.Block())

        @block.sync
        def _(sp):
            def load_x(b):
                sp.dma_start(xa[:], x_v[bass.ds(b, 1)].rearrange("a p n c -> (a p) n c")).then_inc(x_in, 16)

            def write_parts(b, u):
                sp.wait_ge(lo_made, 2 * b + 1)
                for t in range(PARTS):
                    sp.dma_start(scr_q[u][:, t::PARTS, :], parts[:, 0]).then_inc(scr_written, 16)
                sp.wait_ge(lo_made, 2 * b + 2)
                for t in range(PARTS):
                    sp.dma_start(scr_k[u][:, PARTS * t:PARTS * t + PARTS, :], parts[:, 1]).then_inc(scr_written, 16)

            def read_rows(b, u):
                sp.wait_ge(scr_written, 16 * 2 * PARTS * b + 16 * 2 * PARTS)
                for g in range(NG):
                    for dst, scr in ((qx[u], scr_q[u]), (kx[u], scr_k[u])):
                        src = scr[g * HG * D:(g + 1) * HG * D].rearrange("(h d) e t -> (d e) h t", h=HG)
                        sp.dma_start(dst[0:KQ, g * HG:(g + 1) * HG, :], src).then_inc(qk_loaded[u][g], 16)

            def load_negmax(m, u, g):
                sp.wait_ge(nm_copied, m + 1)
                for t in range(PARTS):
                    for f in range(2):
                        h = g * HG + 2 * f
                        sp.dma_start(qx[u][KZ + t:KZ + t + 1, h:h + 2, :].rearrange("p e (i q) -> p (e i) q", q=64),
                                     nm_T[t * 2 * QG:(t + 1) * 2 * QG, 64 * f:64 * f + 64]).then_inc(nm_loaded, 16)

            for u in range(2):
                sp.sem_inc(out_stored[u], 16)
            load_x(0)
            sp.dma_start(wqkv[:], w_qkv).then_inc(w_in, 16)
            sp.wait_ge(xt_made, 1)
            load_x(1)
            for n, w in enumerate((w_gate, w_up)):
                sp.dma_start(wraw[:, n, :].rearrange("p (c d) -> p c d", c=HC),
                             w.rearrange("(c p) d -> p c d", p=P)).then_inc(wff_in, 16)
            sp.dma_start(wraw[:, 2, :], w_down).then_inc(wff_in, 16)
            write_parts(0, 0)
            sp.wait_ge(zeroed, 3)
            sp.wait_ge(ones_made, 1)
            read_rows(0, 0)
            write_parts(1, 1)
            sp.wait_ge(zeroed, 4)
            sp.wait_ge(ones_made, 2)
            read_rows(1, 1)
            load_negmax(0, 0, 0)
            load_negmax(1, 0, 1)

            def body(i, u, prep, more):
                b = 2 * i + u
                if prep:
                    sp.wait_ge(xt_made, b + 2)
                    load_x(b + 2)
                x_b = x_v[bass.ds(b, 1)].rearrange("a p n c -> (a p) n c")
                sp.dma_start(res[:, bass.ds(NB * b, NB), :], x_b).then_inc(res_in, 16)
                for n in range(NG):
                    if more or n + 2 < NG:
                        load_negmax(NG * b + n + 2, fills(i, u, n + 2)[1], (n + 2) % NG)
                    if n == 2 and prep:
                        for g in range(NG):
                            sp.wait_ge(qk_loaded[u][g], 32 * fills(i, u, 0)[0])
                        write_parts(b + 2, u)
                if prep:
                    sp.wait_ge(st_full, SLOTS * NG * b + SLOTS * NG)
                    read_rows(b + 2, u)

            bodies(sp, body)

            with sp.Fori(0, B // 2) as i:
                for u in range(2):
                    sp.wait_ge(yo_made, NB * 2 * i + NB * (u + 1))
                    sp.dma_start(out_v[bass.ds(2 * i + u, 1)].rearrange("a p n c -> (a p) n c"),
                                 yo[u][:]).then_inc(out_stored[u], 16)
            for u in range(2):
                sp.wait_ge(out_stored[u], 16 + 16 * (B // 2))

        @block.tensor
        def _(pe):
            free = [None]

            def take_misc(then):
                if free[0] is not None:
                    pe.wait_ge(*free[0])
                free[0] = then

            def transposes4(dst, src):
                for n in range(NB):
                    last = pe.transpose(dst[:, P * n:P * n + P], src[:, P * n:P * n + P], identf[:])
                return last

            def turn_x(b):
                pe.wait_ge(x_in, 16 * b + 16)
                take_misc((xt_copied, b + 1))
                transposes4(misc, xa[:].rearrange("p n c -> p (n c)")).then_inc(xt_made, 1)

            def project_qk(b, n):
                pe.wait_ge(xt_copied, b + 1)
                take_misc((rest_made, 2 * b + n + 1))
                pe.matmul(misc, wqkv[:, C * n:C * n + C], xT[:], start=True, stop=True).then_inc((q_made, k_made)[n], 1)

            def project_v(b):
                pe.wait_ge(xt_copied, b + 1)
                take_misc((v_copied, b + 1))
                for n in range(NB):
                    last = pe.matmul(misc[:, C * n:C * n + C], xT[:, P * n:P * n + P], wqkv[:, 2 * C:3 * C],
                                     start=True, stop=True)
                last.then_inc(v_made, 1)

            def turn_negmax(m):
                pe.wait_ge(nm_split, m + 1)
                take_misc((nm_copied, m + 1))
                pe.transpose(misc[:, 0:P // 2].bitcast(BF16),
                             nm_parts[:].rearrange("p t c -> p (t c)"), identb[:]).then_inc(nm_turned, 1)

            def turn_out(G):
                pe.wait_ge(ot_copied, G + 2)
                take_misc((attn_made, G + 2))
                transposes4(misc, oT[:]).then_inc(o_turned, 1)

            def score_slot(G, u, g, s):
                if s == 0:
                    pe.wait_ge(nm_loaded, NM_DMAS * G + NM_DMAS)
                if not (isinstance(G, int) and G == 0 and s < 2):
                    pe.wait_ge(exp_done, SLOTS * G + s - 1)
                for bank in (2 * s, 2 * s + 1):
                    blocks = [(h, j) for h in range(HG) for j in range(NB) if key_block_place(h, j)[0] == bank]
                    for n, (h, j) in enumerate(blocks):
                        col, width = key_block_place(h, j)[1], T - P * j
                        last = pe.matmul(st_ps[(g * SLOTS + s) % 2][:, bank % 2, col:col + width],
                                         kx[u][0:KS, HG * g + h, P * j:P * j + P],
                                         qx[u][0:KS, HG * g + h, P * j:T], start=(n == 0),
                                         stop=(n == len(blocks) - 1), skip_group_check=True)
                last.then_inc(st_full, 1)

            def max_bank(M, u, g, filled, bank):
                if bank == 0:
                    pe.wait_ge(qk_loaded[u][g], 32 * filled)
                if not (isinstance(M, int) and MX_BANKS * M + bank < 2):
                    pe.wait_ge(mx_reduced, MX_BANKS * M + bank - 1)
                segments = max_segments(bank)
                for n, (pair, i, col) in enumerate(segments):
                    for f in range(2):
                        h, width = HG * g + pair + 2 * f, 64 * (i + 1)
                        last = pe.matmul(mx_ps[(MX_BANKS * g + bank) % 2][64 * f:64 * f + 64, col:col + width],
                                         qx[u][0:KZ, h, 64 * i:64 * i + 64], kx[u][0:KZ, h, 0:width],
                                         start=(n == 0), stop=(n == len(segments) - 1), skip_group_check=True)
                last.then_inc(mx_full, 1)

            def values(G, b, u, g, j):
                if j == 0:
                    pe.wait_ge(v_copied, b + 1)
                    pe.wait_ge(ot_copied, G + 1)
                pe.wait_ge(diag_done, NB * G + (1, 2, 4, 3)[j])
                if j == 0:
                    pe.wait_ge(exp_done, SLOTS * G + SLOTS)
                for h in range(HG):
                    bank, col = key_block_place(h, j)
                    last = pe.matmul(pv_ps[VW * h:VW * h + VW, P * j:T], vx[u][:, j, HG * g + h, :],
                                     pt[g % 2][:, bank, col:col + T - P * j], start=(j == 0), stop=(j == NB - 1),
                                     skip_group_check=True)
                if j == NB - 1:
                    last.then_inc(pv_done, 1)

            pe.sem_inc(pv_done, 1)
            pe.sem_inc(o_turned, 1)
            pe.wait_ge(const_made, 4)
            turn_x(0)
            pe.wait_ge(w_in, 16)
            project_qk(0, 0)
            project_qk(0, 1)
            project_v(0)
            turn_x(1)
            project_qk(1, 0)
            project_qk(1, 1)
            pe.wait_ge(wff_deq, 3)
            for n in range(3):
                take_misc((wff_copied, n + 1))
                for c in range(HC):
                    last = pe.transpose(misc[:, P * c:P * c + P], wdeq[:, n, P * c:P * c + P], identf[:])
                last.then_inc(wff_turned, 1)

            for M in range(LAG):
                for bank in range(MX_BANKS):
                    max_bank(M, 0, M, 1, bank)
                if M == 0:
                    turn_negmax(0)
            for s in range(SLOTS):
                score_slot(0, 0, 0, s)
                for bank in range(2 * s, min(2 * s + 2, MX_BANKS)):
                    max_bank(LAG, 0, LAG, 1, bank)
                if s == 1:
                    turn_negmax(1)
            free[0] = None

            def body(i, u, prep, more):
                b = 2 * i + u
                for n in range(NG if more else NG - 1):
                    G = NG * b + n + 1
                    for s in range(SLOTS):
                        score_slot(G, fills(i, u, n + 1)[1], (n + 1) % NG, s)
                        if more or n + 1 + LAG < NG:
                            filled, um = fills(i, u, n + 1 + LAG)
                            max_bank(G + LAG, um, (n + 1 + LAG) % NG, filled, 2 * s)
                        if s < NB:
                            values(G - 1, b, u, n, s)
                        if s == 0 and n == 2 and prep:
                            project_qk(b + 2, 0)
                        if s == 1 and (more or n + 2 < NG):
                            if n == 0:
                                pe.wait_ge(nm_copied, G + 1)
                                pe.wait_ge(attn_made, NG * b + 1)
                            turn_negmax(G + 1)
                        if s == 2:
                            if n == 0 and more:
                                project_v(b + 1)
                            if n == 1 and prep:
                                turn_x(b + 2)
                            if n == 2 and prep:
                                project_qk(b + 2, 1)
                        if (more or n + 1 + LAG < NG) and 2 * s + 1 < MX_BANKS:
                            max_bank(G + LAG, um, (n + 1 + LAG) % NG, filled, 2 * s + 1)
                        if s == SLOTS - 1:
                            turn_out(G - 1)
                free[0] = None

            bodies(pe, body)
            for j in range(NB):
                values(NG * B - 1, B - 1, 1, NG - 1, j)
            pe.wait_ge(attn_made, NG * B)
            turn_out(NG * B - 1)

            def turn_x1(c, u):
                pe.wait_ge(x1_made, NB * c + NB)
                if not (isinstance(c, int) and c == 0):
                    pe.wait_ge(x1t_copied, c)
                transposes4(psum[:, 0, :], x1[u][:].rearrange("p n c -> p (n c)")).then_inc(x1_turned, 1)

            def ffn(c, u, first, last_one):
                pe.wait_ge(x1t_copied, c + 1)
                for m in range(HC):
                    k = HC * u + m
                    if not (first and m < 2):
                        pe.wait_ge(silu_done, HC * c + m - 1)
                        pe.wait_ge(hid_made, HC * c + m - 1)
                    pe.matmul(psum[:, 1 + k % 2, :], wT[:, 0, P * m:P * m + P], x1T[u][:],
                              start=True, stop=True).then_inc(gate_full, 1)
                    pe.matmul(psum[:, 3 + k % 2, :], wT[:, 1, P * m:P * m + P], x1T[u][:],
                              start=True, stop=True).then_inc(up_full, 1)
                if not last_one:
                    turn_x1(c + 1, 1 - u)
                if not first:
                    pe.wait_ge(r2_made, c)
                for m in range(HC):
                    pe.wait_ge(hid_made, HC * c + m + 1)
                    for n in range(NB):
                        last = pe.matmul(psum[:, 5, C * n:C * n + C], hid[:, m, P * n:P * n + P],
                                         wT[:, 2, P * m:P * m + P], start=(m == 0 and n == 0),
                                         stop=(m == HC - 1 and n == NB - 1), skip_group_check=True)
                last.then_inc(y_full, 1)

            pe.wait_ge(wff_copied, 3)
            turn_x1(0, 0)
            whole_batches(pe, ffn)

        @block.scalar
        def _(act):
            copy = ACT.Copy

            def copy_xt(b):
                act.wait_ge(xt_made, b + 1)
                if not (isinstance(b, int) and b == 0):
                    act.wait_ge(k_made, b)
                    act.wait_ge(v_made, b)
                act.activation(xT[:], misc, copy).then_inc(xt_copied, 1)

            def first_part(b, n):
                act.wait_ge((q_made, k_made)[n], b + 1)
                if not (isinstance(b, int) and b == 0):
                    act.wait_ge(scr_written, 16 * 2 * PARTS * b)
                act.activation(parts[:, n, 0, :], misc, copy).then_inc(hi_made, 1)

            def copy_v(b, u):
                act.wait_ge(v_made, b + 1)
                if not (isinstance(b, int) and b < 2):
                    act.wait_ge(pv_done, NG * b - NG + 1)
                act.activation(vx[u][:, :, :, 0:D], misc.rearrange("p (n h d) -> p n h d", n=NB, h=H),
                               copy).then_inc(v_copied, 1)

            def exp_slot(G, g, s):
                act.wait_ge(st_full, SLOTS * G + s + 1)
                if s == 0 and not (isinstance(G, int) and G < 2):
                    act.wait_ge(pv_done, G)
                act.activation(pt[g % 2][:, 2 * s:2 * s + 2, :], st_ps[(g * SLOTS + s) % 2], ACT.Exp,
                               scale=SM_SCALE).then_inc(exp_done, 1)

            def copy_negmax(m):
                act.wait_ge(nm_turned, m + 1)
                if not (isinstance(m, int) and m == 0):
                    act.wait_ge(nm_loaded, NM_DMAS * m)
                act.activation(nm_T[:], misc[0:PARTS * HG * NB, 0:P // 2].bitcast(BF16), copy).then_inc(nm_copied, 1)

            def copy_out(G):
                act.wait_ge(pv_done, G + 2)
                act.wait_ge(o_turned, G + 1)
                act.activation(oT[:], pv_ps, copy).then_inc(ot_copied, 1)

            act.sem_inc(ot_copied, 1)
            copy_xt(0)
            first_part(0, 0)
            first_part(0, 1)
            act.wait_ge(v_ones, 2)
            copy_v(0, 0)
            copy_xt(1)
            first_part(1, 0)
            first_part(1, 1)
            for n in range(3):
                act.wait_ge(wff_turned, n + 1)
                act.activation(wT[:, n, :], misc[:, 0:HID], copy).then_inc(wff_copied, 1)
            copy_negmax(0)
            for s in range(SLOTS):
                exp_slot(0, 0, s)
                if s == 1:
                    copy_negmax(1)

            def body(i, u, prep, more):
                b = 2 * i + u
                for n in range(NG if more else NG - 1):
                    G = NG * b + n + 1
                    for s in range(SLOTS):
                        exp_slot(G, (n + 1) % NG, s)
                        if s == 0 and n == 2 and prep:
                            first_part(b + 2, 0)
                        if s == 1 and (more or n + 2 < NG):
                            copy_negmax(G + 1)
                        if s == 2:
                            if n == 0 and more:
                                copy_v(b + 1, 1 - u)
                            if n == 1 and prep:
                                copy_xt(b + 2)
                            if n == 2 and prep:
                                first_part(b + 2, 1)
                        if s == 3:
                            copy_out(G - 1)

            bodies(act, body)
            copy_out(NG * B - 1)

            def copy_x1t(c, u):
                act.wait_ge(x1_turned, c + 1)
                if not (isinstance(c, int) and c < 2):
                    act.wait_ge(up_full, HC * c - HC)
                act.activation(x1T[u][:], psum[:, 0, :], copy).then_inc(x1t_copied, 1)

            def ffn(c, u, first, last_one):
                for m in range(HC):
                    k = HC * u + m
                    act.wait_ge(gate_full, HC * c + m + 1)
                    if not (first and m < 2):
                        act.wait_ge(hid_made, HC * c + m - 1)
                    act.activation(sg[k % 2][:], psum[:, 1 + k % 2, :], ACT.Silu).then_inc(silu_done, 1)
                if not last_one:
                    copy_x1t(c + 1, 1 - u)

            copy_x1t(0, 0)
            whole_batches(act, ffn)

        @block.vector
        def _(dve):
            def rest(b, n):
                dve.wait_ge(hi_made, 2 * b + n + 1)
                if not (isinstance(b, int) and b == 0 and n == 0):
                    dve.wait_ge(lo_made, 2 * b + n)
                dve.tensor_tensor(r1[:], misc, parts[:, n, 0, :], ALU.subtract).then_inc(rest_made, 1)

            def reduce_bank(M, g, bank):
                if bank == 0 and not (isinstance(M, int) and M < 2):
                    dve.wait_ge(nm_split, M - 1)
                dve.wait_ge(mx_full, MX_BANKS * M + bank + 1)
                dve.sem_inc(dve_gate, 1)
                for pair, i, col in max_segments(bank):
                    width = 64 * (i + 1)
                    seg = mx_ps[(MX_BANKS * g + bank) % 2][:, col:col + width]
                    last = dve.tensor_tensor_reduce(seg, seg, mask[:, T - width:T], -1.0, -MASKED, ALU.add, ALU.min,
                                                    negmax[g % 2][:, QG * pair + i:QG * pair + i + 1])
                last.then_inc(mx_reduced, 1)

            def normalise(G, g):
                dve.wait_ge(o_turned, G + 2)
                turned = misc.rearrange("p (r w) -> p r w", w=VW)
                dve.reciprocal(rsum[:], turned[:, :, D]).then_inc(rs_made, 1)
                if g == 0 and not (isinstance(G, int) and G == 0):
                    dve.wait_ge(res_made, res_count(G) + 1)
                dve.wait_ge(rs_made, G + 1)
                dve.tensor_tensor(attn[:, :, HG * g:HG * g + HG, :],
                                  misc.rearrange("p (n h w) -> p n h w", n=NB, h=HG)[:, :, :, 0:D],
                                  rsum[:].rearrange("p (n h) -> p n h", n=NB).unsqueeze(3)
                                  .to_broadcast([P, NB, HG, D]), ALU.mult).then_inc(attn_made, 1)

            batch = [0]

            def res_count(G):
                return batch[0]

            dve.sem_inc(attn_made, 1)
            def make_ones(u):
                dve.memset(kx[u][64:P].bitcast(F32), BF16_ONES).then_inc(ones_made, 1)

            def split_qk(b, n):
                rest(b, n)
                dve.wait_ge(rest_made, 2 * b + n + 1)
                dve.tensor_scalar(parts[:, n, 1, :], r1[:], 1.0, 0.0, ALU.mult, ALU.add).then_inc(mid_made, 1)
                dve.wait_ge(mid_made, 2 * b + n + 1)
                dve.tensor_tensor(parts[:, n, 2, :], r1[:], parts[:, n, 1, :], ALU.subtract).then_inc(lo_made, 1)

            make_ones(0)
            for n in range(2):
                split_qk(0, n)
            for u in range(2):
                dve.wait_ge(v_zeroed, u + 1)
                dve.memset(vx[u][:, :, :, D:D + 1], 1.0).then_inc(v_ones, 1)
            for n in range(2):
                split_qk(1, n)
            make_ones(1)
            dve.wait_ge(const_made, 4)
            for M in range(LAG):
                for bank in range(MX_BANKS):
                    reduce_bank(M, M, bank)
            for bank in range(MX_BANKS):
                reduce_bank(LAG, LAG, bank)

            def body(i, u, prep, more):
                b = 2 * i + u
                batch[0] = b
                for n in range(NG if more else NG - 1):
                    G = NG * b + n + 1
                    for s in range(SLOTS):
                        if more or n + 1 + LAG < NG:
                            for bank in range(2 * s, min(2 * s + 2, MX_BANKS)):
                                reduce_bank(G + LAG, (n + 1 + LAG) % NG, bank)
                        if n == 2 and prep and s in (0, 2):
                            rest(b + 2, s // 2)
                    normalise(G - 1, n)

            bodies(dve, body)

            def norm_stats(src, k, st_made, mv_made, count):
                for n in range(NB):
                    dve.bn_stats(stats[:, k, n, :], src(n)).then_inc(st_made, 1)
                dve.wait_ge(st_made, count)
                dve.sem_inc(dve_gate, 1)
                for n in range(NB):
                    dve.bn_aggr(mv[:, k, n, :], stats[:, k, n, :]).then_inc(mv_made, 1)

            def stats1(c):
                dve.wait_ge(res_made, c + 2)
                if not (isinstance(c, int) and c == 0):
                    dve.wait_ge(ve1_made, c)
                    dve.wait_ge(x1_made, NB * c)
                norm_stats(lambda n: res[:, bass.ds(NB * c + n, 1), :].rearrange("p a c -> p (a c)"), 0, st1_made,
                           mv1_made, NB * c + NB)

            def norm1(c, u):
                dve.wait_ge(rstd1_made, c + 1)
                if not (isinstance(c, int) and c < 2):
                    dve.wait_ge(x1_turned, c - 1)
                    dve.wait_ge(r2_made, c - 1)
                for n in range(NB):
                    dve.tensor_scalar(x1[u][:, n, :], res[:, bass.ds(NB * c + n, 1), :].rearrange("p a c -> p (a c)"),
                                      mv[:, 0, n, 0:1], rstd[:, 0, n:n + 1], ALU.subtract, ALU.mult).then_inc(x1_made, 1)

            def ffn(c, u, first, last_one):
                for m in range(HC):
                    k = HC * u + m
                    dve.wait_ge(silu_done, HC * c + m + 1)
                    dve.wait_ge(up_full, HC * c + m + 1)
                    if not first and m == 0:
                        dve.wait_ge(y_full, c)
                    dve.tensor_tensor(hid[:, m, :], psum[:, 3 + k % 2, :], sg[k % 2][:], ALU.mult).then_inc(hid_made, 1)
                    if m == 0 and not last_one:
                        norm1(c + 1, 1 - u)
                if not (last_one or isinstance(c, int) and c == B - 2):
                    stats1(c + 2)
                dve.wait_ge(y_full, c + 1)
                if not first:
                    dve.wait_ge(yo_made, NB * c)
                dve.tensor_tensor(r2[:].rearrange("p n c -> p (n c)"), psum[:, 5, :],
                                  x1[u][:].rearrange("p n c -> p (n c)"), ALU.add).then_inc(r2_made, 1)
                dve.wait_ge(r2_made, c + 1)
                norm_stats(lambda n: r2[:, n, :], 1, st2_made, mv2_made, NB * c + NB)

            stats1(0)
            norm1(0, 0)
            stats1(1)
            normalise(NG * B - 1, NG - 1)
            whole_batches(dve, ffn)

        @block.gpsimd
        def _(pool):
            pool.sem_inc(res_made, 1)
            pool.memset(identf[:], 0.0).then_inc(zeroed, 1)
            pool.memset(mask[:], 0.0).then_inc(zeroed, 1)
            pool.wait_ge(zeroed, 2)
            pool.affine_select(out=identf[:], in_=identf[:], pattern=[[-1, P]], compare_op=ALU.not_equal, fill=1.0,
                               base=0, channel_multiplier=1).then_inc(const_made, 1)
            for f in range(2):
                tri = mask[64 * f:64 * f + 64, T - 64:T]
                pool.wait_ge(const_made, 1 + f)
                pool.affine_select(out=tri, in_=tri, pattern=[[-1, 64]], compare_op=ALU.is_ge, fill=MASKED,
                                   base=0, channel_multiplier=1).then_inc(const_made, 1)
            pool.wait_ge(const_made, 3)
            pool.tensor_scalar(identb[:], identf[:], 1.0, 0.0, ALU.mult, ALU.add).then_inc(const_made, 1)
            for u in range(2):
                if u == 1:
                    pool.wait_ge(zeroed, 3)
                pool.memset(vx[u][:], 0.0).then_inc(v_zeroed, 1)
                pool.wait_ge(v_zeroed, u + 1)
                pool.memset(qx[u][64:KZ].bitcast(F32), 0.0).then_inc(zeroed, 1)
            pool.wait_ge(zeroed, 4)
            pool.memset(minus_half[:], -0.5).then_inc(v_zeroed, 1)
            pool.memset(nm_parts[:], 0.0).then_inc(v_zeroed, 1)
            pool.wait_ge(v_zeroed, 4)

            def split_qk(b, n):
                pool.wait_ge(rest_made, 2 * b + n + 1)
                pool.sem_inc(pool_gate, 1)
                pool.tensor_scalar(parts[:, n, 1, :], r1[:], 1.0, 0.0, ALU.mult, ALU.add).then_inc(mid_made, 1)
                pool.wait_ge(mid_made, 2 * b + n + 1)
                pool.tensor_tensor(parts[:, n, 2, :], r1[:], parts[:, n, 1, :], ALU.subtract).then_inc(lo_made, 1)

            def split_negmax(M, g):
                nm = negmax[g % 2][:]
                pool.wait_ge(mx_reduced, MX_BANKS * M + MX_BANKS)
                if not (isinstance(M, int) and M == 0):
                    pool.wait_ge(nm_turned, M)
                pool.sem_inc(pool_gate, 1)
                pool.tensor_scalar(nm_parts[:, 0, :], nm, 1.0, 0.0, ALU.mult, ALU.add).then_inc(nm_hi, 1)
                pool.wait_ge(nm_hi, M + 1)
                pool.tensor_tensor(nm_rest[g % 2][:], nm, nm_parts[:, 0, :], ALU.subtract).then_inc(nm_rst, 1)
                pool.wait_ge(nm_rst, M + 1)
                pool.sem_inc(pool_gate, 1)
                pool.tensor_scalar(nm_parts[:, 1, :], nm_rest[g % 2][:], 1.0, 0.0, ALU.mult, ALU.add).then_inc(nm_mid, 1)
                pool.wait_ge(nm_mid, M + 1)
                pool.tensor_tensor(nm_parts[:, 2, :], nm_rest[g % 2][:], nm_parts[:, 1, :],
                                   ALU.subtract).then_inc(nm_split, 1)

            def clear_diagonal(G, g, s):
                for j in {1: (0,), 3: (1, 3), 4: (2,)}[s]:
                    bank, col = key_block_place(0, j)
                    step = 256 if j == 2 else 512
                    blocks = (pt[g % 2][:].rearrange("p b q -> p (b q)")[:, 512 * bank:512 * bank + HG * step]
                              .rearrange("p (h q) -> p h q", h=HG)[:, :, col:col + P])
                    pool.wait_ge(exp_done, SLOTS * G + s + 1)
                    pool.sem_inc(pool_gate, 1)
                    pool.affine_select(out=blocks, in_=blocks, pattern=[[0, HG], [1, P]], compare_op=ALU.is_ge,
                                       fill=0.0, base=0, channel_multiplier=-1).then_inc(diag_done, 1)

            def add_attention(b):
                pool.wait_ge(res_in, 16 * b + 16)
                pool.wait_ge(attn_made, NG * b + NG + 1)
                x_b = res[:, bass.ds(NB * b, NB), :]
                pool.tensor_tensor(x_b, x_b, attn[:].rearrange("p n h d -> p n (h d)"), ALU.add).then_inc(res_made, 1)

            pool.wait_ge(wff_in, 48)
            for n in range(3):
                pool.tensor_scalar(wdeq[:, n, :], wraw[:, n, :], W_SCALE, 0.0, ALU.mult, ALU.add).then_inc(wff_deq, 1)
            split_negmax(0, 0)
            split_negmax(1, 1)
            clear_diagonal(0, 0, 1)
            clear_diagonal(0, 0, 3)
            clear_diagonal(0, 0, 4)
            split_negmax(2, 0)

            def body(i, u, prep, more):
                b = 2 * i + u
                for n in range(NG if more else NG - 1):
                    G = NG * b + n + 1
                    if n == 2 and prep:
                        split_qk(b + 2, 0)
                    clear_diagonal(G, (n + 1) % NG, 1)
                    clear_diagonal(G, (n + 1) % NG, 3)
                    if n == 2 and prep:
                        split_qk(b + 2, 1)
                    clear_diagonal(G, (n + 1) % NG, 4)
                    if more or n + 1 + LAG < NG:
                        split_negmax(G + LAG, (n + 1 + LAG) % NG)
                if more:
                    add_attention(b)

            bodies(pool, body)

            def inverse_deviation(c, k, mv_made, ve_made, rstd_made):
                pool.wait_ge(mv_made, NB * c + NB)
                pool.sem_inc(pool_gate, 1)
                pool.tensor_scalar(veps[:, k, :], mv[:, k, :, 1], 1.0, EPS, ALU.mult, ALU.add).then_inc(ve_made, 1)
                pool.wait_ge(ve_made, c + 1)
                pool.tensor_tensor(rstd[:, k, :], veps[:, k, :], minus_half[:], ALU.pow).then_inc(rstd_made, 1)

            def norm2(c, u):
                pool.wait_ge(rstd2_made, c + 1)
                if not (isinstance(c, int) and c < 2):
                    pool.wait_ge(out_stored[u], 8 * (c - u) + 16)
                pool.sem_inc(pool_gate, 1)
                for n in range(NB):
                    pool.tensor_scalar(yo[u][:, n, :], r2[:, n, :], mv[:, 1, n, 0:1], rstd[:, 1, n:n + 1],
                                       ALU.subtract, ALU.mult).then_inc(yo_made, 1)

            def ffn(c, u, first, last_one):
                if not (last_one or isinstance(c, int) and c == B - 2):
                    inverse_deviation(c + 2, 0, mv1_made, ve1_made, rstd1_made)
                inverse_deviation(c, 1, mv2_made, ve2_made, rstd2_made)
                norm2(c, u)

            inverse_deviation(0, 0, mv1_made, ve1_made, rstd1_made)
            inverse_deviation(1, 0, mv1_made, ve1_made, rstd1_made)
            add_attention(B - 1)
            whole_batches(pool, ffn)


_INS = ["L0_attn_x", "L0_attn_w_qkv", "L0_ffn_w_gate", "L0_ffn_w_up", "L0_ffn_w_down"]


def kernel(**inputs):
    import numpy as np
    import concourse.bacc as bacc
    from concourse.bass_utils import run_bass_kernel_spmd

    nc = bacc.Bacc("TRN2", target_bir_lowering=False, num_devices=1)
    arrays, args = {}, []
    for name in _INS:
        a = np.ascontiguousarray(inputs[name])
        arrays[name] = a
        args.append(nc.dram_tensor(name, a.shape, mybir.dt.from_np(a.dtype), kind="ExternalInput").ap())
    out = nc.dram_tensor("out", (B, T, C), F32, kind="ExternalOutput").ap()
    attention_ffn(nc, *args, out)
    return run_bass_kernel_spmd(nc, [arrays], core_ids=[0]).results[0]["out"]
```
